# Optimizing a Trainium2 kernel written in Bass

```python
import numpy as np
import jax
import jax.numpy as jnp

def _softmax(x, axis=-1):
    return jax.nn.softmax(x, axis=axis)

def _gelu(x):
    return jax.nn.gelu(x, approximate=True)

def _silu(x):
    return jax.nn.silu(x)

def _sigmoid(x):
    return jax.nn.sigmoid(x)

def _layernorm(x, axis=-1, eps=1e-05):
    m = jnp.mean(x, axis=axis, keepdims=True)
    v = jnp.var(x, axis=axis, keepdims=True)
    return (x - m) / jnp.sqrt(v + eps)

def _scatter_add(tgt, idx, src, axis=0):
    return tgt.at[idx].add(src)

def _segment_sum(src, seg, n):
    return jax.ops.segment_sum(src, seg, n)
kernel_name = 'mk_sandwich_d1_jaxref_r8_9827c4'

def setup_inputs(seed: int=0):
    np.random.seed(seed)
    _w = jnp.asarray

    def _L0_attn_setup():
        import jax, jax.numpy as jnp
        import numpy as np
        B, T, D = (4, 256, 128)
        H, Dh = (16, 64)
        key = jax.random.key(seed)
        ks = jax.random.split(key, 5)
        std_qkv = float(np.sqrt(2.0 / (Dh * D)))
        std_o = float(np.sqrt(2.0 / (D * Dh)))
        return {'x': jax.random.normal(ks[0], (B, T, D), dtype=jnp.float32), 'W_Q': jax.random.normal(ks[1], (H, Dh, D), dtype=jnp.float32) * std_qkv, 'b_Q': jnp.zeros((H, Dh), dtype=jnp.float32), 'W_K': jax.random.normal(ks[2], (H, Dh, D), dtype=jnp.float32) * std_qkv, 'b_K': jnp.zeros((H, Dh), dtype=jnp.float32), 'W_V': jax.random.normal(ks[3], (H, Dh, D), dtype=jnp.float32) * std_qkv, 'b_V': jnp.zeros((H, Dh), dtype=jnp.float32), 'W_O': jax.random.normal(ks[4], (H, D, Dh), dtype=jnp.float32) * std_o, 'b_O': jnp.zeros((D,), dtype=jnp.float32)}
    _L0_attn_in = _L0_attn_setup()

    def _L0_ffn_setup():
        import jax, jax.numpy as jnp
        import numpy as np
        key = jax.random.key(seed)
        ks = jax.random.split(key, 5)
        B, S, D_in, D_out, E, R = (4, 128, 128, 128, 8, 16)
        x = jax.random.normal(ks[0], (B, S, D_in), dtype=jnp.float32)
        weight = jax.random.normal(ks[1], (D_out, D_in), dtype=jnp.float32) / np.sqrt(D_in)
        gate_w = jax.random.normal(ks[2], (E, D_in), dtype=jnp.float32) / np.sqrt(D_in)
        lora_U = jax.random.normal(ks[3], (E, R, D_in), dtype=jnp.float32) / np.sqrt(D_in)
        lora_V = jax.random.normal(ks[4], (E, D_out, R), dtype=jnp.float32) / np.sqrt(R)
        return {'x': x, 'weight': weight, 'gate_w': gate_w, 'lora_U': lora_U, 'lora_V': lora_V}
    _L0_ffn_in = _L0_ffn_setup()
    _d = {'L0_attn_x': _L0_attn_in['x'], 'L0_attn_W_Q': _L0_attn_in['W_Q'], 'L0_attn_b_Q': _L0_attn_in['b_Q'], 'L0_attn_W_K': _L0_attn_in['W_K'], 'L0_attn_b_K': _L0_attn_in['b_K'], 'L0_attn_W_V': _L0_attn_in['W_V'], 'L0_attn_b_V': _L0_attn_in['b_V'], 'L0_attn_W_O': _L0_attn_in['W_O'], 'L0_attn_b_O': _L0_attn_in['b_O'], 'L0_ffn_weight': _L0_ffn_in['weight'], 'L0_ffn_gate_w': _L0_ffn_in['gate_w'], 'L0_ffn_lora_U': _L0_ffn_in['lora_U'], 'L0_ffn_lora_V': _L0_ffn_in['lora_V']}
    _x0 = _d['L0_attn_x']
    _d['L0_attn_x'] = jax.random.normal(jax.random.fold_in(jax.random.key(seed), 1), (32, 256, 128), dtype=_x0.dtype)
    del _x0
    return _d

def reference(L0_attn_x, L0_attn_W_Q, L0_attn_b_Q, L0_attn_W_K, L0_attn_b_K, L0_attn_W_V, L0_attn_b_V, L0_attn_W_O, L0_attn_b_O, L0_ffn_weight, L0_ffn_gate_w, L0_ffn_lora_U, L0_ffn_lora_V):

    def _L0_attn_ref(x, W_Q, b_Q, W_K, b_K, W_V, b_V, W_O, b_O):
        import jax, jax.numpy as jnp
        import numpy as np
        B, T, D = (4, 256, 128)
        H, Dh = (16, 64)
        Q = jnp.einsum('btd,hkd->bthk', x, W_Q) + b_Q
        K = jnp.einsum('btd,hkd->bthk', x, W_K) + b_K
        V = jnp.einsum('btd,hkd->bthk', x, W_V) + b_V
        d_head = W_Q.shape[1]
        scores = jnp.einsum('bqhk,bshk->bhqs', Q, K) / jnp.sqrt(jnp.asarray(d_head, x.dtype))
        attn = jax.nn.softmax(scores, axis=-1)
        out_h = jnp.einsum('bhqs,bshk->bqhk', attn, V)
        return jnp.einsum('bqhk,hdk->bqd', out_h, W_O) + b_O

    def _L0_ffn_ref(x, weight, gate_w, lora_U, lora_V):
        import jax, jax.numpy as jnp
        import numpy as np
        scaling = 1.0 / lora_U.shape[1]
        B, S, D_in = x.shape
        xt = x.reshape(-1, D_in)
        gate = jax.nn.softmax(xt @ gate_w.T, axis=-1)
        base = xt @ weight.T
        t = jnp.einsum('nh,erh->ner', xt, lora_U)
        lora = jnp.einsum('ne,eor,ner->no', gate, lora_V, t)
        out = base + scaling * lora
        return out.reshape(B, S, -1)
    x = L0_attn_x
    x = x + _layernorm(_L0_attn_ref(_layernorm(x, axis=-1), L0_attn_W_Q, L0_attn_b_Q, L0_attn_W_K, L0_attn_b_K, L0_attn_W_V, L0_attn_b_V, L0_attn_W_O, L0_attn_b_O), axis=-1)
    x = x + _layernorm(_L0_ffn_ref(_layernorm(x, axis=-1), L0_ffn_weight, L0_ffn_gate_w, L0_ffn_lora_U, L0_ffn_lora_V), axis=-1)
    return x

_drawn_inputs = setup_inputs


def setup_inputs(seed=0):
    import zlib

    import numpy as np

    out = dict(_drawn_inputs(seed))
    spreads = {'L0_attn_b_Q': (0.0, 0.8),
     'L0_attn_b_K': (0.0, 0.8),
     'L0_attn_b_V': (0.0, 0.1),
     'L0_attn_b_O': (0.0, 0.1)}
    factors = {'L0_attn_W_Q': 8.0,
     'L0_attn_W_K': 8.0,
     'L0_ffn_gate_w': 4.701,
     'L0_ffn_lora_U': 3.008,
     'L0_ffn_lora_V': 2.95}
    for name, (base, spread) in spreads.items():
        noise = np.random.default_rng([zlib.crc32(name.encode()), seed]).standard_normal(out[name].shape)
        drawn = base * np.exp(spread * noise) if base else spread * noise
        out[name] = jnp.asarray(drawn.astype(out[name].dtype))
    for name, factor in factors.items():
        out[name] = (out[name] * factor).astype(out[name].dtype)
    return out
```

```python
import concourse.bass as bass
from concourse import mybir
from contextlib import ExitStack

F32 = mybir.dt.float32
F32R = mybir.dt.float32r
ALU = mybir.AluOpType
ACT = mybir.ActivationFunctionType
AX = mybir.AxisListType

B, T, D = 32, 256, 128
H, DH = 16, 64
E, R = 8, 16
P = 128
NT = T // P
PAIRS = H * DH // P
HALF = H * DH // 2
TG = E * R + E
EPS = 1e-5
SCORE_SCALE = DH ** -0.5
LORA_SCALE = 1.0 / R
FIRST_X = 4

B_Q, B_K, B_V, B_O = 0, PAIRS, 2 * PAIRS, 3 * PAIRS
F_W, F_TG, F_V = 0, D, D + TG

FIRST, MIDDLE, LAST, DRAIN = range(4)


def after(engine, sem, count):
    if not (isinstance(count, int) and count <= 0):
        engine.wait_ge(sem, count)


def transformer_layer(nc, x, w_q, w_k, w_v, w_o, biases, ffn_w, out):
    ctx = ExitStack()
    with ctx:
        def sb(name, shape, dt=F32):
            return ctx.enter_context(nc.sbuf_tensor(name, shape, dt))

        def bank(name):
            return ctx.enter_context(nc.psum_tensor(name, [P, 512], F32))

        def sem(name):
            return ctx.enter_context(nc.semaphore(name))

        stage = {n: sb(f"stage_{n}", [P, H * DH]) for n in "qkvo"}
        w_hi = {n: sb(f"w{n}_hi", [P, H * DH], F32R) for n in "qkvo"}
        w_lo = {n: sb(f"w{n}_lo", [P, H * DH], F32R) for n in "qkvo"}
        bias = sb("bias", [P, 3 * PAIRS + 1])
        ffn = sb("ffn", [P, D + TG + D])
        ident = sb("ident", [P, P])
        neg_half = sb("neg_half", [P, NT])

        x_all = sb("x_all", [P, B * NT * D])
        xn = sb("xn", [P, NT * D])
        xt_hi = sb("xt_hi", [P, T], F32R)
        xt_lo = sb("xt_lo", [P, T], F32R)
        q_hi = [sb(f"q_hi{n}", [P, T], F32R) for n in range(2)]
        q_lo = [sb(f"q_lo{n}", [P, T], F32R) for n in range(2)]
        k_hi = [sb(f"k_hi{n}", [P, T], F32R) for n in range(2)]
        k_lo = [sb(f"k_lo{n}", [P, T], F32R) for n in range(2)]
        v_sb = sb("v_sb", [P, NT, H * DH])
        probs = [[sb(f"probs{n}{h}", [P, NT, T]) for h in range(2)] for n in range(2)]
        probs_t = [[sb(f"probs_t{n}{h}", [P, NT, T]) for h in range(2)] for n in range(2)]
        neg_max = [[sb(f"neg_max{n}{h}", [P, NT]) for h in range(2)] for n in range(2)]
        row_sum = [[sb(f"row_sum{n}{h}", [P, NT]) for h in range(2)] for n in range(2)]
        inv_sum = [[sb(f"inv_sum{n}{h}", [P, NT]) for h in range(2)] for n in range(2)]
        o_hi = sb("o_hi", [P, PAIRS, T], F32R)
        o_lo = sb("o_lo", [P, PAIRS, T], F32R)
        yt = sb("yt", [P, T])
        y = sb("y", [P, NT * D])
        x1 = sb("x1", [P, NT * D])
        x1n = sb("x1n", [P, NT * D])
        x1t = sb("x1t", [P, T])
        tg = sb("tg", [P, NT, TG])
        gate_neg_max = sb("gate_neg_max", [P, NT])
        gate_exp = sb("gate_exp", [P, NT, E])
        gate_sum = sb("gate_sum", [P, NT])
        gate_inv = sb("gate_inv", [P, NT])
        gate = sb("gate", [P, NT, E])
        u = sb("u", [P, NT * E * R])
        ut = sb("ut", [P, T])
        z = sb("z", [P, NT * D])
        out_sb = sb("out_sb", [P, NT * D])
        stats = [sb(f"stats{n}", [P, NT, 6]) for n in range(4)]
        stats_seen = sb("stats_seen", [P, 1])
        mean_var = [sb(f"mean_var{n}", [P, NT, 2]) for n in range(4)]
        var_eps = [sb(f"var_eps{n}", [P, NT]) for n in range(4)]
        rstd = [sb(f"rstd{n}", [P, NT]) for n in range(4)]

        scores_ps = [[bank(f"scores{n}{h}") for h in range(2)] for n in range(2)]
        probs_t_ps = [bank(f"probs_t_ps{h}") for h in range(2)]
        bank_a = bank("bank_a")
        bank_b = bank("bank_b")

        x_loaded = [sem(f"x_loaded{n}") for n in range(2)]
        w_loaded = {n: sem(f"w_loaded_{n}") for n in "qkvo"}
        bias_loaded = sem("bias_loaded")
        ffn_loaded = sem("ffn_loaded")
        zeroed = sem("zeroed")
        constants_ready = sem("constants_ready")
        bias_scaled = sem("bias_scaled")
        w_hi_ready = {n: sem(f"w_hi_ready_{n}") for n in "qkvo"}
        w_lo_ready = {n: sem(f"w_lo_ready_{n}") for n in "qkvo"}
        ffn_scaled = sem("ffn_scaled")
        qk_projected = sem("qk_projected")
        qk_hi_ready = sem("qk_hi_ready")
        qk_lo_ready = sem("qk_lo_ready")
        o_projected = sem("o_projected")
        o_hi_ready = sem("o_hi_ready")
        o_lo_ready = sem("o_lo_ready")
        probs_t_copied = [sem(f"probs_t_copied{h}") for h in range(2)]
        scores_ready = sem("scores_ready")
        max_ready = sem("max_ready")
        exp_ready = sem("exp_ready")
        inv_ready = sem("inv_ready")
        probs_ready = sem("probs_ready")
        probs_transposed = sem("probs_transposed")
        xn_centred = sem("xn_centred")
        xn_ready = sem("xn_ready")
        x_transposed = sem("x_transposed")
        xt_hi_ready = sem("xt_hi_ready")
        xt_lo_ready = sem("xt_lo_ready")
        v_projected = sem("v_projected")
        v_copied_act = sem("v_copied_act")
        v_copied_dve = sem("v_copied_dve")
        yt_projected = sem("yt_projected")
        yt_ready = sem("yt_ready")
        y_transposed = sem("y_transposed")
        y_copied = sem("y_copied")
        y_normed = sem("y_normed")
        x1_ready = sem("x1_ready")
        x1n_ready = sem("x1n_ready")
        x1_transposed = sem("x1_transposed")
        x1t_ready = sem("x1t_ready")
        tg_projected = sem("tg_projected")
        tg_copied = sem("tg_copied")
        gate_max_ready = sem("gate_max_ready")
        gate_exp_ready = sem("gate_exp_ready")
        gate_inv_ready = sem("gate_inv_ready")
        gate_ready = sem("gate_ready")
        u_ready = sem("u_ready")
        u_transposed = sem("u_transposed")
        ut_ready = sem("ut_ready")
        z_projected = sem("z_projected")
        z_copied = sem("z_copied")
        z_centred = sem("z_centred")
        z_normed = sem("z_normed")
        out_ready = sem("out_ready")
        out_stored = sem("out_stored")
        stats_ready = [sem(f"stats_ready{n}") for n in range(4)]
        mean_var_ready = [sem(f"mean_var_ready{n}") for n in range(4)]
        var_eps_ready = [sem(f"var_eps_ready{n}") for n in range(4)]
        rstd_ready = [sem(f"rstd_ready{n}") for n in range(4)]
        LN_X, LN_Y, LN_X1, LN_Z = range(4)

        def tile(buffer, j):
            return buffer[:, j * P:(j + 1) * P]

        def x_tiles(b):
            return x_all[:, bass.ds(b * (NT * D), NT * D)]

        def head_rows(h):
            return slice(h * DH, (h + 1) * DH)

        def pair_cols(pair):
            return slice(pair * P, (pair + 1) * P)

        def has_scores(mode):
            return mode != DRAIN

        def has_trailing(p, mode, lag):
            return p < lag if mode == DRAIN else not (mode == FIRST and p < lag)

        def has_next_qk(p, mode):
            return mode != DRAIN and (p + 2 < PAIRS or mode != LAST)

        def has_next(mode):
            return mode in (FIRST, MIDDLE)

        def has_previous(mode):
            return mode != FIRST

        def run(engine, body):
            body(0, FIRST)
            with engine.Fori(1, B - 1) as i:
                body(i, MIDDLE)
            body(B - 1, LAST)
            body(B, DRAIN)

        block = ctx.enter_context(nc.Block())

        @block.sync
        def _(sp):
            x_v = x.rearrange("b (p j) d -> p b (j d)", j=NT)
            out_v = out.rearrange("b (p j) d -> p b (j d)", j=NT)
            x_sb = x_all[:, :].rearrange("p (b n) -> p b n", b=B)
            sp.dma_start(x_sb[:, 0:FIRST_X, :], x_v[:, 0:FIRST_X, :]).then_inc(x_loaded[0], 16)
            sp.dma_start(stage["q"][:, :], w_q).then_inc(w_loaded["q"], 16)
            sp.dma_start(stage["k"][:, :], w_k).then_inc(w_loaded["k"], 16)
            sp.dma_start(bias[:, :], biases).then_inc(bias_loaded, 16)
            sp.dma_start(stage["v"][:, :], w_v).then_inc(w_loaded["v"], 16)
            sp.dma_start(stage["o"][:, :], w_o).then_inc(w_loaded["o"], 16)
            sp.dma_start(ffn[:, :], ffn_w).then_inc(ffn_loaded, 16)
            sp.dma_start(x_sb[:, FIRST_X:B, :], x_v[:, FIRST_X:B, :]).then_inc(x_loaded[1], 16)
            with sp.Fori(0, B) as b:
                sp.wait_ge(out_ready, b + 1)
                sp.dma_start(out_v[:, bass.ds(b, 1), :].rearrange("p b n -> p (b n)"),
                             out_sb[:, :]).then_inc(out_stored, 16)
            sp.wait_ge(out_stored, 16 * B)

        @block.tensor
        def _(pe):
            def project_qk(pair):
                for n, w in enumerate("qk"):
                    dst = bank_a[:, n * T:(n + 1) * T]
                    cols = pair_cols(pair)
                    nc.tensor.matmul(dst, w_hi[w][:, cols], xt_hi[:, :], start=True, stop=False)
                    nc.tensor.matmul(dst, w_hi[w][:, cols], xt_lo[:, :], start=False, stop=False)
                    last = nc.tensor.matmul(dst, w_lo[w][:, cols], xt_hi[:, :], start=False, stop=True)
                last.then_inc(qk_projected, 1)

            def transpose_tiles(dst, src):
                for j in range(NT):
                    last = nc.tensor.transpose(tile(dst, j), tile(src, j), ident[:, :])
                return last

            def project_v(dst, j, half):
                cols = slice(half * HALF, (half + 1) * HALF)
                nc.tensor.matmul(dst[:, :], tile(xt_hi, j), w_hi["v"][:, cols], start=True, stop=False)
                nc.tensor.matmul(dst[:, :], tile(xt_hi, j), w_lo["v"][:, cols], start=False, stop=False)
                nc.tensor.matmul(dst[:, :], tile(xt_lo, j), w_hi["v"][:, cols], start=False,
                                 stop=True).then_inc(v_projected, 1)

            pe.wait_ge(constants_ready, 1)
            pe.wait_ge(xn_ready, 1)
            transpose_tiles(bank_a, xn).then_inc(x_transposed, 1)
            pe.wait_ge(w_lo_ready["q"], 1)
            pe.wait_ge(w_lo_ready["k"], 1)
            for pair in range(2):
                if pair == 0:
                    pe.wait_ge(xt_lo_ready, 1)
                else:
                    pe.wait_ge(qk_lo_ready, 1)
                project_qk(pair)
            pe.wait_ge(w_lo_ready["v"], 1)
            pe.wait_ge(w_lo_ready["o"], 1)
            pe.wait_ge(ffn_scaled, 1)

            def body(i, mode):
                for p in range(PAIRS):
                    g = PAIRS * i + p
                    par = p % 2
                    last_pair = min(p + 1, PAIRS - 1) if mode == LAST else p + 1
                    bank_a_free = (qk_lo_ready, PAIRS * i + last_pair + 1)
                    if mode == DRAIN:
                        bank_a_free = (z_copied, B - 1)
                    bank_b_free = (o_lo_ready, g - 2)
                    if mode == DRAIN:
                        bank_b_free = (o_lo_ready, PAIRS * B + min(p - 2, 0))

                    if has_scores(mode):
                        after(pe, qk_lo_ready, g + 1)
                        after(pe, exp_ready, 2 * (g - 1))
                        for j in range(NT):
                            for n, (a, b) in enumerate(((q_hi, k_hi), (q_hi, k_lo), (q_lo, k_hi))):
                                for h in range(2):
                                    last = nc.tensor.matmul(
                                        scores_ps[par][h][:, j * T:(j + 1) * T],
                                        tile(a[par], j)[head_rows(h), :], b[par][head_rows(h), :],
                                        start=(n == 0), stop=(n == 2))
                                    if j == NT - 1 and n == 2:
                                        last.then_inc(scores_ready, 1)

                    if p == 0 and has_scores(mode):
                        pe.wait_ge(*bank_a_free)
                        project_v(bank_a, 0, 0)
                        bank_a_free = (v_copied_act, 2 * i + 1)
                    if p == 2 and has_previous(mode):
                        pe.wait_ge(*bank_a_free)
                        pe.wait_ge(o_lo_ready, PAIRS * i)
                        for pair in range(PAIRS):
                            cols = pair_cols(pair)
                            for n, (w, o) in enumerate(((w_hi, o_hi), (w_hi, o_lo), (w_lo, o_hi))):
                                last = nc.tensor.matmul(
                                    bank_a[:, 0:T], w["o"][:, cols], o[:, pair, :],
                                    start=(pair == 0 and n == 0), stop=(pair == PAIRS - 1 and n == 2))
                        last.then_inc(yt_projected, 1)
                        bank_a_free = (yt_ready, i)
                    if p == 3 and has_scores(mode):
                        pe.wait_ge(*bank_a_free)
                        project_v(bank_a, 1, 1)
                        bank_a_free = (v_copied_act, 2 * i + 2)
                    if p == 5 and has_previous(mode):
                        pe.wait_ge(*bank_a_free)
                        pe.wait_ge(x1n_ready, i)
                        transpose_tiles(bank_a, x1n).then_inc(x1_transposed, 1)
                        bank_a_free = (x1t_ready, i)
                    if p == 6 and has_next(mode):
                        pe.wait_ge(*bank_a_free)
                        pe.wait_ge(xn_ready, i + 2)
                        transpose_tiles(bank_a, xn).then_inc(x_transposed, 1)
                        bank_a_free = (xt_lo_ready, i + 2)
                    if p == 7 and has_previous(mode):
                        pe.wait_ge(*bank_a_free)
                        pe.wait_ge(ut_ready, i)
                        for j in range(NT):
                            nc.tensor.matmul(tile(bank_a, j), tile(x1t, j), ffn[:, F_W:F_W + D],
                                             start=True, stop=False)
                            last = nc.tensor.matmul(tile(bank_a, j), tile(ut, j), ffn[:, F_V:F_V + D],
                                                    start=False, stop=True)
                        last.then_inc(z_projected, 1)
                        bank_a_free = (z_copied, i)

                    if has_trailing(p, mode, 1):
                        for h in range(2):
                            pe.wait_ge(probs_ready, 2 * (g - 1) + h + 1)
                            after(pe, probs_t_copied[h], g - 1)
                            for j in range(NT):
                                for s in range(NT):
                                    last = nc.tensor.transpose(
                                        probs_t_ps[h][:, s * T + j * P:s * T + (j + 1) * P],
                                        probs[1 - par][h][:, j, s * P:(s + 1) * P], ident[:, :])
                            last.then_inc(probs_transposed, 1)

                    if p == 0 and has_scores(mode):
                        after(pe, *bank_b_free)
                        project_v(bank_b, 1, 0)
                        bank_b_free = (v_copied_dve, 2 * i + 1)
                    if p == 2 and has_scores(mode):
                        after(pe, *bank_b_free)
                        project_v(bank_b, 0, 1)
                        bank_b_free = (v_copied_dve, 2 * i + 2)
                    if p == 3 and has_previous(mode):
                        pe.wait_ge(*bank_b_free)
                        pe.wait_ge(yt_ready, i)
                        transpose_tiles(bank_b, yt).then_inc(y_transposed, 1)
                        bank_b_free = (y_copied, i)
                    if p == 5 and has_previous(mode):
                        pe.wait_ge(*bank_b_free)
                        pe.wait_ge(x1t_ready, i)
                        for j in range(NT):
                            last = nc.tensor.matmul(bank_b[:, j * TG:(j + 1) * TG], tile(x1t, j),
                                                    ffn[:, F_TG:F_TG + TG], start=True, stop=True)
                        last.then_inc(tg_projected, 1)
                        bank_b_free = (tg_copied, i)
                    if p == 6 and has_previous(mode):
                        pe.wait_ge(*bank_b_free)
                        pe.wait_ge(u_ready, i)
                        transpose_tiles(bank_b, u).then_inc(u_transposed, 1)
                        bank_b_free = (ut_ready, i)

                    if has_next_qk(p, mode):
                        if p == PAIRS - 2:
                            pe.wait_ge(xt_lo_ready, i + 2)
                        pe.wait_ge(*bank_a_free)
                        project_qk((p + 2) % PAIRS)

                    if has_trailing(p, mode, 2):
                        pair = (p - 2) % PAIRS
                        for h in range(2):
                            pe.wait_ge(probs_t_copied[h], g - 1)
                        after(pe, *bank_b_free)
                        if p == 2:
                            pe.wait_ge(v_copied_act, 2 * i + 1)
                            pe.wait_ge(v_copied_dve, 2 * i + 1)
                        if p == 6:
                            pe.wait_ge(v_copied_act, 2 * i + 2)
                            pe.wait_ge(v_copied_dve, 2 * i + 2)
                        for s in range(NT):
                            for h in range(2):
                                last = nc.tensor.matmul(
                                    bank_b[head_rows(h), 0:T],
                                    v_sb[:, s, pair * P + h * DH:pair * P + (h + 1) * DH],
                                    probs_t[par][h][:, s, :], start=(s == 0), stop=(s == NT - 1))
                        last.then_inc(o_projected, 1)

            run(pe, body)

        @block.scalar
        def _(act):
            def qk_hi(pair, par, g):
                act.wait_ge(qk_projected, g + 1)
                nc.scalar.activation(q_hi[par][:, :], bank_a[:, 0:T], ACT.Identity,
                                     bias=bias[:, B_Q + pair:B_Q + pair + 1])
                nc.scalar.activation(k_hi[par][:, :], bank_a[:, T:2 * T], ACT.Identity,
                                     bias=bias[:, B_K + pair:B_K + pair + 1]).then_inc(qk_hi_ready, 1)

            act.wait_ge(bias_loaded, 16)
            nc.scalar.mul(bias[:, B_Q:B_Q + PAIRS], bias[:, B_Q:B_Q + PAIRS],
                          SCORE_SCALE).then_inc(bias_scaled, 1)
            for n in "qk":
                act.wait_ge(w_loaded[n], 16)
                nc.scalar.mul(w_hi[n][:, :], stage[n][:, :],
                              SCORE_SCALE if n == "q" else 1.0).then_inc(w_hi_ready[n], 1)
            act.wait_ge(x_transposed, 1)
            nc.scalar.copy(xt_hi[:, :], bank_a[:, 0:T]).then_inc(xt_hi_ready, 1)
            for n in "vo":
                act.wait_ge(w_loaded[n], 16)
                nc.scalar.copy(w_hi[n][:, :], stage[n][:, :]).then_inc(w_hi_ready[n], 1)
            act.wait_ge(ffn_loaded, 16)
            nc.scalar.mul(ffn[:, F_V:F_V + D], ffn[:, F_V:F_V + D], LORA_SCALE).then_inc(ffn_scaled, 1)
            act.wait_ge(bias_scaled, 1)
            for pair in range(2):
                qk_hi(pair, pair, pair)

            def body(i, mode):
                for p in range(PAIRS):
                    g = PAIRS * i + p
                    par = p % 2

                    def exponentials(h):
                        act.wait_ge(max_ready, 2 * g + h + 1)
                        after(act, probs_transposed, 2 * (g - 2) + h + 1)
                        for j in range(NT):
                            last = nc.scalar.activation(
                                probs[par][h][:, j, :], scores_ps[par][h][:, j * T:(j + 1) * T],
                                ACT.Exp, bias=neg_max[par][h][:, j:j + 1],
                                accum_out=row_sum[par][h][:, j:j + 1])
                        last.then_inc(exp_ready, 1)

                    if has_trailing(p, mode, 3):
                        pair = (p - 3) % PAIRS
                        act.wait_ge(o_projected, g - 2)
                        nc.scalar.activation(o_hi[:, pair, :], bank_b[:, 0:T], ACT.Identity,
                                             bias=bias[:, B_V + pair:B_V + pair + 1]
                                             ).then_inc(o_hi_ready, 1)
                    if p == 6 and has_next(mode):
                        act.wait_ge(x_transposed, i + 2)
                        nc.scalar.copy(xt_hi[:, :], bank_a[:, 0:T]).then_inc(xt_hi_ready, 1)
                    if has_scores(mode):
                        exponentials(0)
                    if p == 0 and has_scores(mode):
                        act.wait_ge(v_projected, 4 * i + 1)
                        nc.scalar.copy(v_sb[:, 0, 0:HALF], bank_a[:, :]).then_inc(v_copied_act, 1)
                    if p == 2 and has_previous(mode):
                        if has_scores(mode):
                            exponentials(1)
                        act.wait_ge(yt_projected, i)
                        nc.scalar.activation(yt[:, :], bank_a[:, 0:T], ACT.Identity,
                                             bias=bias[:, B_O:B_O + 1]).then_inc(yt_ready, 1)
                    if p == 3 and has_scores(mode):
                        act.wait_ge(v_projected, 4 * i + 4)
                        nc.scalar.copy(v_sb[:, 1, HALF:2 * HALF], bank_a[:, :]).then_inc(v_copied_act, 1)
                    if p == 5 and has_previous(mode):
                        act.wait_ge(x1_transposed, i)
                        nc.scalar.copy(x1t[:, :], bank_a[:, 0:T]).then_inc(x1t_ready, 1)
                    if has_trailing(p, mode, 1):
                        act.wait_ge(probs_transposed, 2 * (g - 1) + 1)
                        after(act, o_projected, g - 2)
                        nc.scalar.copy(probs_t[1 - par][0][:, :, :].rearrange("p s q -> p (s q)"),
                                       probs_t_ps[0][:, :]).then_inc(probs_t_copied[0], 1)
                    if p == 6 and has_previous(mode):
                        act.wait_ge(u_transposed, i)
                        nc.scalar.copy(ut[:, :], bank_b[:, 0:T]).then_inc(ut_ready, 1)
                    if has_scores(mode) and not (p == 2 and has_previous(mode)):
                        exponentials(1)
                    if p == 5 and has_previous(mode):
                        act.wait_ge(gate_max_ready, i)
                        for j in range(NT):
                            last = nc.scalar.activation(gate_exp[:, j, :], tg[:, j, E * R:TG], ACT.Exp,
                                                        bias=gate_neg_max[:, j:j + 1],
                                                        accum_out=gate_sum[:, j:j + 1])
                        last.then_inc(gate_exp_ready, 1)
                    if has_next_qk(p, mode):
                        qk_hi((p + 2) % PAIRS, par, g + 2)

            run(act, body)

        @block.vector
        def _(dve):
            def f32(ap):
                return ap.bitcast(F32)

            def qk_lo(pair, par, g):
                dve.wait_ge(qk_hi_ready, g + 1)
                nc.vector.scalar_tensor_tensor(q_lo[par][:, :], bank_a[:, 0:T],
                                               bias[:, B_Q + pair:B_Q + pair + 1],
                                               f32(q_hi[par][:, :]), ALU.add, ALU.subtract)
                nc.vector.scalar_tensor_tensor(k_lo[par][:, :], bank_a[:, T:2 * T],
                                               bias[:, B_K + pair:B_K + pair + 1],
                                               f32(k_hi[par][:, :]), ALU.add, ALU.subtract
                                               ).then_inc(qk_lo_ready, 1)

            def ln_stats(ln, src, count):
                for j in range(NT):
                    last = nc.vector.bn_stats(stats[ln][:, j, :], tile(src, j))
                last.then_inc(stats_ready[ln], 1)
                dve.wait_ge(stats_ready[ln], count)
                nc.vector.tensor_copy(stats_seen[:, :], stats[ln][:, NT - 1, 0:1])
                for j in range(NT):
                    last = nc.vector.bn_aggr(mean_var[ln][:, j, :], stats[ln][:, j, :])
                last.then_inc(mean_var_ready[ln], 1)
                dve.wait_ge(mean_var_ready[ln], count)
                nc.vector.tensor_scalar(var_eps[ln][:, :], mean_var[ln][:, :, 1], EPS, None,
                                        ALU.add).then_inc(var_eps_ready[ln], 1)

            def ln_apply(ln, dst, src):
                for j in range(NT):
                    last = nc.vector.tensor_scalar(tile(dst, j), tile(src, j), mean_var[ln][:, j, 0:1],
                                                   rstd[ln][:, j:j + 1], ALU.subtract, ALU.mult)
                return last

            dve.wait_ge(x_loaded[0], 16)
            ln_stats(LN_X, x_all[:, 0:NT * D], 1)
            for n in "qk":
                dve.wait_ge(w_hi_ready[n], 1)
                nc.vector.scalar_tensor_tensor(w_lo[n][:, :], stage[n][:, :],
                                               SCORE_SCALE if n == "q" else 1.0, f32(w_hi[n][:, :]),
                                               ALU.mult, ALU.subtract).then_inc(w_lo_ready[n], 1)
            dve.wait_ge(xt_hi_ready, 1)
            nc.vector.tensor_tensor(xt_lo[:, :], bank_a[:, 0:T], f32(xt_hi[:, :]),
                                    ALU.subtract).then_inc(xt_lo_ready, 1)
            for n in "vo":
                dve.wait_ge(w_hi_ready[n], 1)
                nc.vector.tensor_tensor(w_lo[n][:, :], stage[n][:, :], f32(w_hi[n][:, :]),
                                        ALU.subtract).then_inc(w_lo_ready[n], 1)
            for pair in range(2):
                qk_lo(pair, pair, pair)

            def body(i, mode):
                for p in range(PAIRS):
                    g = PAIRS * i + p
                    par = p % 2
                    if has_trailing(p, mode, 3):
                        pair = (p - 3) % PAIRS
                        dve.wait_ge(o_hi_ready, g - 2)
                        nc.vector.scalar_tensor_tensor(o_lo[:, pair, :], bank_b[:, 0:T],
                                                       bias[:, B_V + pair:B_V + pair + 1],
                                                       f32(o_hi[:, pair, :]), ALU.add, ALU.subtract
                                                       ).then_inc(o_lo_ready, 1)
                    if p == 4 and has_previous(mode):
                        dve.wait_ge(rstd_ready[LN_Y], i)
                        ln_apply(LN_Y, y, y).then_inc(y_normed, 1)
                        dve.wait_ge(y_normed, i)
                        nc.vector.tensor_tensor(x1[:, :], y[:, :], x_tiles(i - 1),
                                                ALU.add).then_inc(x1_ready, 1)
                    if p == 5 and has_previous(mode):
                        dve.wait_ge(rstd_ready[LN_X1], i)
                        ln_apply(LN_X1, x1n, x1).then_inc(x1n_ready, 1)
                    if p == 6 and has_previous(mode):
                        dve.wait_ge(gate_exp_ready, i)
                        nc.vector.reciprocal(gate_inv[:, :], gate_sum[:, :]).then_inc(gate_inv_ready, 1)
                        dve.wait_ge(gate_inv_ready, i)
                        for j in range(NT):
                            last = nc.vector.tensor_scalar(gate[:, j, :], gate_exp[:, j, :],
                                                           gate_inv[:, j:j + 1], None, ALU.mult)
                        last.then_inc(gate_ready, 1)
                        dve.wait_ge(gate_ready, i)
                        for j in range(NT):
                            last = nc.vector.tensor_tensor(
                                tile(u, j).rearrange("p (e r) -> p e r", e=E),
                                tg[:, j, 0:E * R].rearrange("p (e r) -> p e r", e=E),
                                gate[:, j, :].unsqueeze(2).to_broadcast([P, E, R]), ALU.mult)
                        last.then_inc(u_ready, 1)

                    if has_scores(mode):
                        for h in range(2):
                            dve.wait_ge(scores_ready, 2 * g + h + 1)
                            nc.vector.tensor_reduce(
                                neg_max[par][h][:, :],
                                scores_ps[par][h][:, :].rearrange("p (j s) -> p j s", j=NT),
                                AX.X, ALU.max, negate=True).then_inc(max_ready, 1)
                    if p == 1 and has_next(mode):
                        if mode == MIDDLE:
                            dve.wait_ge(x_loaded[1], 16)
                        ln_stats(LN_X, x_tiles(i + 1), i + 2)
                    if p == 4 and has_previous(mode):
                        dve.wait_ge(x1_ready, i)
                        ln_stats(LN_X1, x1, i)
                    if p == 6 and has_next(mode):
                        dve.wait_ge(xt_hi_ready, i + 2)
                        nc.vector.tensor_tensor(xt_lo[:, :], bank_a[:, 0:T], f32(xt_hi[:, :]),
                                                ALU.subtract).then_inc(xt_lo_ready, 1)
                    if p == 7 and has_previous(mode):
                        dve.wait_ge(z_projected, i)
                        nc.vector.tensor_copy(z[:, :], bank_a[:, 0:T]).then_inc(z_copied, 1)
                    if has_trailing(p, mode, 1):
                        dve.wait_ge(probs_transposed, 2 * (g - 1) + 2)
                        after(dve, o_projected, g - 2)
                        nc.vector.tensor_copy(probs_t[1 - par][1][:, :, :].rearrange("p s q -> p (s q)"),
                                              probs_t_ps[1][:, :]).then_inc(probs_t_copied[1], 1)
                    if p == 0 and has_scores(mode):
                        dve.wait_ge(v_projected, 4 * i + 2)
                        nc.vector.tensor_copy(v_sb[:, 1, 0:HALF], bank_b[:, :]).then_inc(v_copied_dve, 1)
                    if p == 2 and has_scores(mode):
                        dve.wait_ge(v_projected, 4 * i + 3)
                        nc.vector.tensor_copy(v_sb[:, 0, HALF:2 * HALF],
                                              bank_b[:, :]).then_inc(v_copied_dve, 1)
                    if p == 3 and has_previous(mode):
                        dve.wait_ge(y_transposed, i)
                        nc.vector.tensor_copy(y[:, :], bank_b[:, 0:T]).then_inc(y_copied, 1)
                        dve.wait_ge(y_copied, i)
                        ln_stats(LN_Y, y, i)
                    if p == 5 and has_previous(mode):
                        dve.wait_ge(tg_projected, i)
                        nc.vector.tensor_copy(tg[:, :, :].rearrange("p j n -> p (j n)"),
                                              bank_b[:, 0:NT * TG]).then_inc(tg_copied, 1)
                        dve.wait_ge(tg_copied, i)
                        nc.vector.tensor_reduce(gate_neg_max[:, :], tg[:, :, E * R:TG], AX.X, ALU.max,
                                                negate=True).then_inc(gate_max_ready, 1)
                    if has_scores(mode):
                        for h in range(2):
                            dve.wait_ge(exp_ready, 2 * g + h + 1)
                            nc.vector.reciprocal(inv_sum[par][h][:, :],
                                                 row_sum[par][h][:, :]).then_inc(inv_ready, 1)
                    if p == 7 and has_previous(mode):
                        dve.wait_ge(z_copied, i)
                        ln_stats(LN_Z, z, i)
                    if has_next_qk(p, mode):
                        qk_lo((p + 2) % PAIRS, par, g + 2)

            run(dve, body)

        @block.gpsimd
        def _(pool):
            def per_tile(column):
                return column.unsqueeze(2).to_broadcast([P, NT, D])

            def tiles(ap):
                return ap.rearrange("p (j d) -> p j d", j=NT)

            def ln_rstd(ln, count):
                pool.wait_ge(var_eps_ready[ln], count)
                nc.gpsimd.tensor_tensor(rstd[ln][:, :], var_eps[ln][:, :], neg_half[:, :],
                                        ALU.pow).then_inc(rstd_ready[ln], 1)

            def norm_x(b):
                ln_rstd(LN_X, b + 1)
                nc.gpsimd.tensor_tensor(tiles(xn[:, :]), tiles(x_tiles(b)),
                                        per_tile(mean_var[LN_X][:, :, 0]),
                                        ALU.subtract).then_inc(xn_centred, 1)
                pool.wait_ge(rstd_ready[LN_X], b + 1)
                pool.wait_ge(xn_centred, b + 1)
                nc.gpsimd.tensor_tensor(tiles(xn[:, :]), tiles(xn[:, :]), per_tile(rstd[LN_X][:, :]),
                                        ALU.mult).then_inc(xn_ready, 1)

            nc.gpsimd.memset(neg_half[:, :], -0.5)
            nc.gpsimd.memset(ident[:, :], 0.0).then_inc(zeroed, 1)
            pool.wait_ge(zeroed, 1)
            nc.gpsimd.affine_select(out=ident[:, :], in_=ident[:, :], compare_op=ALU.not_equal, fill=1.0,
                                    base=0, pattern=[[-1, P]], channel_multiplier=1
                                    ).then_inc(constants_ready, 1)
            pool.wait_ge(constants_ready, 1)
            norm_x(0)

            def body(i, mode):
                for p in range(PAIRS):
                    g = PAIRS * i + p
                    par = p % 2

                    def scale_probs(h):
                        pool.wait_ge(inv_ready, 2 * g + h + 1)
                        nc.gpsimd.tensor_tensor(
                            probs[par][h][:, :, :], probs[par][h][:, :, :],
                            inv_sum[par][h][:, :].unsqueeze(2).to_broadcast([P, NT, T]),
                            ALU.mult).then_inc(probs_ready, 1)

                    if has_scores(mode):
                        scale_probs(0)
                    if p == 3 and has_previous(mode):
                        ln_rstd(LN_Y, i)
                    if p == 4 and has_previous(mode):
                        ln_rstd(LN_X1, i)
                    if has_scores(mode):
                        scale_probs(1)
                    if p == 1 and has_next(mode):
                        norm_x(i + 1)
                    if p == 7 and has_previous(mode):
                        ln_rstd(LN_Z, i)
                        nc.gpsimd.tensor_tensor(tiles(z[:, :]), tiles(z[:, :]),
                                                per_tile(mean_var[LN_Z][:, :, 0]),
                                                ALU.subtract).then_inc(z_centred, 1)
                        pool.wait_ge(rstd_ready[LN_Z], i)
                        pool.wait_ge(z_centred, i)
                        nc.gpsimd.tensor_tensor(tiles(z[:, :]), tiles(z[:, :]), per_tile(rstd[LN_Z][:, :]),
                                                ALU.mult).then_inc(z_normed, 1)
                        pool.wait_ge(z_normed, i)
                        after(pool, out_stored, 16 * (i - 1))
                        nc.gpsimd.tensor_tensor(out_sb[:, :], z[:, :], x1[:, :],
                                                ALU.add).then_inc(out_ready, 1)

            run(pool, body)


def kernel(L0_attn_x, L0_attn_W_Q, L0_attn_b_Q, L0_attn_W_K, L0_attn_b_K, L0_attn_W_V, L0_attn_b_V,
           L0_attn_W_O, L0_attn_b_O, L0_ffn_weight, L0_ffn_gate_w, L0_ffn_lora_U, L0_ffn_lora_V):
    import numpy as np
    import concourse.bacc as bacc
    from concourse import mybir as mb
    from concourse.bass_utils import run_bass_kernel_spmd

    def head_weight(w):
        return np.asarray(w).reshape(H * DH, D).T

    def head_bias(b):
        return np.asarray(b).reshape(PAIRS, P).T

    laid_out = {
        "x": np.asarray(L0_attn_x),
        "w_q": head_weight(L0_attn_W_Q),
        "w_k": head_weight(L0_attn_W_K),
        "w_v": head_weight(L0_attn_W_V),
        "w_o": np.asarray(L0_attn_W_O).transpose(0, 2, 1).reshape(PAIRS, P, D).transpose(1, 0, 2)
                 .reshape(P, PAIRS * D),
        "biases": np.concatenate([head_bias(L0_attn_b_Q), head_bias(L0_attn_b_K),
                                  head_bias(L0_attn_b_V), np.asarray(L0_attn_b_O).reshape(D, 1)], axis=1),
        "ffn_w": np.concatenate([np.asarray(L0_ffn_weight).T,
                                 np.asarray(L0_ffn_lora_U).reshape(E * R, D).T,
                                 np.asarray(L0_ffn_gate_w).T,
                                 np.asarray(L0_ffn_lora_V).transpose(0, 2, 1).reshape(E * R, D)], axis=1),
    }
    nc = bacc.Bacc("TRN2", target_bir_lowering=False, num_devices=1)
    arrays, args = {}, []
    for name, a in laid_out.items():
        a = np.ascontiguousarray(a)
        arrays[f"in_{name}"] = a
        args.append(nc.dram_tensor(f"in_{name}", a.shape, mb.dt.from_np(a.dtype), kind="ExternalInput").ap())
    out = nc.dram_tensor("out", (B, T, D), mb.dt.float32, kind="ExternalOutput").ap()
    transformer_layer(nc, *args, out)
    return run_bass_kernel_spmd(nc, [arrays], core_ids=[0]).results[0]["out"]
```

```python
import concourse.bass as bass
from concourse import mybir
from contextlib import ExitStack

F32 = mybir.dt.float32
F32R = mybir.dt.float32r
ALU = mybir.AluOpType
ACT = mybir.ActivationFunctionType
AX = mybir.AxisListType

B, T, D = 32, 256, 128
H, DH = 16, 64
E, R = 8, 16
P = 128
NT = T // P
PAIRS = H * DH // P
HALF = H * DH // 2
TG = E * R + E
EPS = 1e-5
SCORE_SCALE = DH ** -0.5
LORA_SCALE = 1.0 / R
UNROLL = 2
assert (B - 2) % UNROLL == 0

B_Q, B_K, B_V, B_O = 0, PAIRS, 2 * PAIRS, 3 * PAIRS
F_W, F_TG, F_V = 0, D, D + TG

FIRST, MIDDLE, LAST, DRAIN = range(4)


def after(engine, sem, count):
    if not (isinstance(count, int) and count <= 0):
        engine.wait_ge(sem, count)


def transformer_layer(nc, x, w_q, w_k, w_v, w_o, biases, ffn_w, out):
    ctx = ExitStack()
    with ctx:
        def sb(name, shape, dt=F32):
            return ctx.enter_context(nc.sbuf_tensor(name, shape, dt))

        def bank(name):
            return ctx.enter_context(nc.psum_tensor(name, [P, 512], F32))

        def sem(name):
            return ctx.enter_context(nc.semaphore(name))

        stage = {n: sb(f"stage_{n}", [P, H * DH]) for n in "qkvo"}
        w_hi = {n: sb(f"w{n}_hi", [P, H * DH], F32R) for n in "qkvo"}
        w_lo = {n: sb(f"w{n}_lo", [P, H * DH], F32R) for n in "qkvo"}
        bias = sb("bias", [P, 3 * PAIRS + 1])
        ffn = sb("ffn", [P, D + TG + D])
        ident = sb("ident", [P, P])
        neg_half = sb("neg_half", [P, NT])

        x_all = sb("x_all", [P, B * NT * D])
        xn = sb("xn", [P, NT * D])
        xt_hi = sb("xt_hi", [P, T], F32R)
        xt_lo = sb("xt_lo", [P, T], F32R)
        q_hi = [sb(f"q_hi{n}", [P, T], F32R) for n in range(2)]
        q_lo = [sb(f"q_lo{n}", [P, T], F32R) for n in range(2)]
        k_hi = [sb(f"k_hi{n}", [P, T], F32R) for n in range(2)]
        k_lo = [sb(f"k_lo{n}", [P, T], F32R) for n in range(2)]
        v_sb = sb("v_sb", [P, NT, H * DH])
        probs = [[sb(f"probs{n}{h}", [P, NT, T]) for h in range(2)] for n in range(2)]
        probs_t = [[sb(f"probs_t{n}{h}", [P, NT, T]) for h in range(2)] for n in range(2)]
        neg_max = [[sb(f"neg_max{n}{h}", [P, NT]) for h in range(2)] for n in range(2)]
        row_sum = [[sb(f"row_sum{n}{h}", [P, NT]) for h in range(2)] for n in range(2)]
        inv_sum = [[sb(f"inv_sum{n}{h}", [P, NT]) for h in range(2)] for n in range(2)]
        o_hi = sb("o_hi", [P, PAIRS, T], F32R)
        o_lo = sb("o_lo", [P, PAIRS, T], F32R)
        yt = sb("yt", [P, T])
        y = sb("y", [P, NT * D])
        x1 = sb("x1", [P, NT * D])
        x1n = sb("x1n", [P, NT * D])
        x1t = sb("x1t", [P, T])
        tg = sb("tg", [P, NT, TG])
        gate_neg_max = sb("gate_neg_max", [P, NT])
        gate_exp = sb("gate_exp", [P, NT, E])
        gate_sum = sb("gate_sum", [P, NT])
        gate_inv = sb("gate_inv", [P, NT])
        gate = sb("gate", [P, NT, E])
        u = sb("u", [P, NT * E * R])
        ut = sb("ut", [P, T])
        z = sb("z", [P, NT * D])
        stats = [sb(f"stats{n}", [P, NT, 6]) for n in range(4)]
        stats_seen = sb("stats_seen", [P, 1])
        mean_var = [sb(f"mean_var{n}", [P, NT, 2]) for n in range(4)]
        var_eps = [sb(f"var_eps{n}", [P, NT]) for n in range(4)]
        rstd = [sb(f"rstd{n}", [P, NT]) for n in range(4)]

        scores_ps = [[bank("scores0")] * 2, [bank("scores10"), bank("scores11")]]
        probs_t_ps = [bank(f"probs_t_ps{h}") for h in range(2)]
        qk_ps = bank("qk_ps")
        o_ps = bank("o_ps")
        extra_ps = bank("extra_ps")

        x_loaded = [sem(f"x_loaded{n}") for n in range(3)]
        early_loaded = {n: sem(f"early_loaded_{n}") for n in "qk"}
        early_hi_ready = {n: sem(f"early_hi_ready_{n}") for n in "qk"}
        early_lo_ready = {n: sem(f"early_lo_ready_{n}") for n in "qk"}
        w_loaded = {n: sem(f"w_loaded_{n}") for n in "qkvo"}
        bias_loaded = sem("bias_loaded")
        ffn_loaded = sem("ffn_loaded")
        zeroed = sem("zeroed")
        constants_ready = sem("constants_ready")
        bias_scaled = sem("bias_scaled")
        w_hi_ready = {n: sem(f"w_hi_ready_{n}") for n in "qkvo"}
        w_lo_ready = {n: sem(f"w_lo_ready_{n}") for n in "qkvo"}
        ffn_scaled = sem("ffn_scaled")
        qk_projected = sem("qk_projected")
        qk_hi_ready = sem("qk_hi_ready")
        qk_lo_ready = sem("qk_lo_ready")
        o_projected = sem("o_projected")
        o_hi_ready = sem("o_hi_ready")
        o_lo_ready = sem("o_lo_ready")
        probs_t_copied = [sem(f"probs_t_copied{h}") for h in range(2)]
        scores_ready = [sem(f"scores_ready{h}") for h in range(2)]
        max_ready = [sem(f"max_ready{h}") for h in range(2)]
        exp_ready = [sem(f"exp_ready{h}") for h in range(2)]
        inv_ready = [sem(f"inv_ready{h}") for h in range(2)]
        probs_ready = [sem(f"probs_ready{h}") for h in range(2)]
        probs_transposed = [sem(f"probs_transposed{h}") for h in range(2)]
        xn_centred = sem("xn_centred")
        xn_ready = sem("xn_ready")
        x_transposed = sem("x_transposed")
        xt_hi_ready = sem("xt_hi_ready")
        xt_lo_ready = sem("xt_lo_ready")
        v_projected = [sem(f"v_projected{n}") for n in range(4)]
        v_copied = [sem(f"v_copied{n}") for n in range(4)]
        yt_projected = sem("yt_projected")
        yt_ready = sem("yt_ready")
        y_transposed = sem("y_transposed")
        y_copied = sem("y_copied")
        y_normed = sem("y_normed")
        x1_ready = sem("x1_ready")
        x1n_ready = sem("x1n_ready")
        x1_transposed = sem("x1_transposed")
        x1t_ready = sem("x1t_ready")
        tg_projected = sem("tg_projected")
        tg_copied = sem("tg_copied")
        gate_max_ready = sem("gate_max_ready")
        gate_exp_ready = sem("gate_exp_ready")
        gate_inv_ready = sem("gate_inv_ready")
        gate_ready = sem("gate_ready")
        u_ready = sem("u_ready")
        u_transposed = sem("u_transposed")
        ut_ready = sem("ut_ready")
        z_projected = sem("z_projected")
        z_copied = sem("z_copied")
        z_centred = sem("z_centred")
        z_normed = sem("z_normed")
        out_ready = sem("out_ready")
        out_stored = sem("out_stored")
        stats_ready = [sem(f"stats_ready{n}") for n in range(4)]
        mean_var_ready = [sem(f"mean_var_ready{n}") for n in range(4)]
        var_eps_ready = [sem(f"var_eps_ready{n}") for n in range(4)]
        rstd_ready = [sem(f"rstd_ready{n}") for n in range(4)]
        LN_X, LN_Y, LN_X1, LN_Z = range(4)

        def tile(buffer, j):
            return buffer[:, j * P:(j + 1) * P]

        def x_tiles(b):
            return x_all[:, bass.ds(b * (NT * D), NT * D)]

        every, early, late = slice(0, PAIRS * P), slice(0, 2 * P), slice(2 * P, PAIRS * P)

        def head_rows(h):
            return slice(h * DH, (h + 1) * DH)

        def pair_cols(pair):
            return slice(pair * P, (pair + 1) * P)

        def has_scores(mode):
            return mode != DRAIN

        def has_trailing(p, mode, lag):
            return p < lag if mode == DRAIN else not (mode == FIRST and p < lag)

        def has_next_qk(p, mode):
            return mode != DRAIN and (p + 2 < PAIRS or mode != LAST)

        def has_next(mode):
            return mode in (FIRST, MIDDLE)

        def has_previous(mode):
            return mode != FIRST

        def run(engine, body):
            body(0, FIRST)
            with engine.Fori(0, (B - 2) // UNROLL) as step:
                for n in range(UNROLL):
                    body(step * UNROLL + 1 + n, MIDDLE)
            body(B - 1, LAST)
            body(B, DRAIN)

        block = ctx.enter_context(nc.Block())

        @block.sync
        def _(sp):
            x_v = x.rearrange("b (p j) d -> p b (j d)", j=NT)
            out_v = out.rearrange("b (p j) d -> p b (j d)", j=NT)
            x_sb = x_all[:, :].rearrange("p (b n) -> p b n", b=B)
            sp.dma_start(x_sb[:, 0:1, :], x_v[:, 0:1, :]).then_inc(x_loaded[0], 16)
            sp.dma_start(bias[:, :], biases).then_inc(bias_loaded, 16)
            for n, w in (("q", w_q), ("k", w_k)):
                sp.dma_start(stage[n][:, early], w[:, early]).then_inc(early_loaded[n], 16)
            sp.dma_start(stage["v"][:, :], w_v).then_inc(w_loaded["v"], 16)
            sp.dma_start(x_sb[:, 1:2, :], x_v[:, 1:2, :]).then_inc(x_loaded[1], 16)
            for n, w in (("q", w_q), ("k", w_k)):
                sp.dma_start(stage[n][:, late], w[:, late]).then_inc(w_loaded[n], 16)
            sp.dma_start(stage["o"][:, :], w_o).then_inc(w_loaded["o"], 16)
            sp.dma_start(ffn[:, :], ffn_w).then_inc(ffn_loaded, 16)
            sp.dma_start(x_sb[:, 2:B, :], x_v[:, 2:B, :]).then_inc(x_loaded[2], 16)
            with sp.Fori(0, B) as b:
                sp.wait_ge(out_ready, b + 1)
                sp.dma_start(out_v[:, bass.ds(b, 1), :].rearrange("p b n -> p (b n)"),
                             x_tiles(b)).then_inc(out_stored, 16)
            sp.wait_ge(out_stored, 16 * B)

        @block.tensor
        def _(pe):
            def project_qk(pair):
                for n, w in enumerate("qk"):
                    dst = qk_ps[:, n * T:(n + 1) * T]
                    cols = pair_cols(pair)
                    nc.tensor.matmul(dst, w_hi[w][:, cols], xt_hi[:, :], start=True, stop=False)
                    nc.tensor.matmul(dst, w_hi[w][:, cols], xt_lo[:, :], start=False, stop=False)
                    last = nc.tensor.matmul(dst, w_lo[w][:, cols], xt_hi[:, :], start=False, stop=True)
                last.then_inc(qk_projected, 1)

            def transpose_tiles(dst, src):
                for j in range(NT):
                    last = nc.tensor.transpose(tile(dst, j), tile(src, j), ident[:, :])
                return last

            def project_v(dst, quarter):
                j, half = quarter % 2, quarter // 2
                cols = slice(half * HALF, (half + 1) * HALF)
                nc.tensor.matmul(dst[:, :], tile(xt_hi, j), w_hi["v"][:, cols], start=True, stop=False)
                nc.tensor.matmul(dst[:, :], tile(xt_hi, j), w_lo["v"][:, cols], start=False, stop=False)
                nc.tensor.matmul(dst[:, :], tile(xt_lo, j), w_hi["v"][:, cols], start=False,
                                 stop=True).then_inc(v_projected[quarter], 1)

            pe.wait_ge(constants_ready, 1)
            pe.wait_ge(xn_ready, 1)
            transpose_tiles(extra_ps, xn).then_inc(x_transposed, 1)
            pe.wait_ge(early_lo_ready["q"], 1)
            pe.wait_ge(early_lo_ready["k"], 1)
            for pair in range(2):
                if pair == 0:
                    pe.wait_ge(xt_lo_ready, 1)
                else:
                    pe.wait_ge(qk_lo_ready, 1)
                project_qk(pair)

            def body(i, mode):
                extra_free = (xt_lo_ready, 1) if mode == FIRST else (z_copied, i)

                for p in range(PAIRS):
                    g = PAIRS * i + p
                    par = p % 2

                    def scores():
                        after(pe, qk_lo_ready, g + 1)
                        after(pe, exp_ready[0], g)
                        for j in range(NT):
                            for n, (a, b) in enumerate(((q_hi, k_hi), (q_hi, k_lo), (q_lo, k_hi))):
                                for h in range(2):
                                    last = nc.tensor.matmul(
                                        scores_ps[h][par][:, j * T:(j + 1) * T],
                                        tile(a[par], j)[head_rows(h), :], b[par][head_rows(h), :],
                                        start=(n == 0), stop=(n == 2))
                                    if j == NT - 1 and n == 2:
                                        last.then_inc(scores_ready[h], 1)

                    def transpose_probs(h):
                        pe.wait_ge(probs_ready[h], g)
                        after(pe, probs_t_copied[h], g - 1)
                        for j in range(NT):
                            for s in range(NT):
                                last = nc.tensor.transpose(
                                    probs_t_ps[h][:, s * T + j * P:s * T + (j + 1) * P],
                                    probs[1 - par][h][:, j, s * P:(s + 1) * P], ident[:, :])
                        last.then_inc(probs_transposed[h], 1)

                    def next_qk():
                        if p == PAIRS - 2:
                            pe.wait_ge(xt_lo_ready, i + 2)
                        pe.wait_ge(qk_lo_ready, g + 2)
                        if mode == FIRST and p == 0:
                            pe.wait_ge(w_lo_ready["q"], 1)
                            pe.wait_ge(w_lo_ready["k"], 1)
                        project_qk((p + 2) % PAIRS)

                    def probs_v():
                        pair = (p - 2) % PAIRS
                        for h in range(2):
                            pe.wait_ge(probs_t_copied[h], g - 1)
                        after(pe, o_lo_ready, g - 2)
                        if pair == 0 or pair == PAIRS // 2:
                            for j in range(NT):
                                pe.wait_ge(v_copied[pair // (PAIRS // 2) * 2 + j], i + 1)
                        for s in range(NT):
                            for h in range(2):
                                last = nc.tensor.matmul(
                                    o_ps[head_rows(h), 0:T],
                                    v_sb[:, s, pair * P + h * DH:pair * P + (h + 1) * DH],
                                    probs_t[par][h][:, s, :], start=(s == 0), stop=(s == NT - 1))
                        last.then_inc(o_projected, 1)

                    def extra_v(quarter):
                        if mode == FIRST:
                            pe.wait_ge(w_lo_ready["v"], 1)
                        pe.wait_ge(*extra_free)
                        project_v(extra_ps, quarter)
                        return v_copied[quarter], i + 1

                    def output_projection(pairs):
                        if pairs[0] == 0:
                            pe.wait_ge(*extra_free)
                        pe.wait_ge(o_lo_ready, PAIRS * (i - 1) + pairs[-1] + 1)
                        for pair in pairs:
                            for n, (w, o) in enumerate(((w_hi, o_hi), (w_hi, o_lo), (w_lo, o_hi))):
                                last = nc.tensor.matmul(
                                    extra_ps[:, 0:T], w["o"][:, pair_cols(pair)], o[:, pair, :],
                                    start=(pair == 0 and n == 0), stop=(pair == PAIRS - 1 and n == 2))
                        if pairs[-1] == PAIRS - 1:
                            last.then_inc(yt_projected, 1)
                        return yt_ready, i

                    def transpose_y():
                        pe.wait_ge(*extra_free)
                        transpose_tiles(extra_ps, yt).then_inc(y_transposed, 1)
                        return y_copied, i

                    def transpose_x1n():
                        pe.wait_ge(*extra_free)
                        pe.wait_ge(x1n_ready, i)
                        transpose_tiles(extra_ps, x1n).then_inc(x1_transposed, 1)
                        return x1t_ready, i

                    def transpose_xn():
                        pe.wait_ge(*extra_free)
                        pe.wait_ge(xn_ready, i + 2)
                        transpose_tiles(extra_ps, xn).then_inc(x_transposed, 1)
                        return xt_lo_ready, i + 2

                    def project_tg():
                        pe.wait_ge(x1t_ready, i)
                        pe.wait_ge(*extra_free)
                        for j in range(NT):
                            last = nc.tensor.matmul(extra_ps[:, j * TG:(j + 1) * TG], tile(x1t, j),
                                                    ffn[:, F_TG:F_TG + TG], start=True, stop=True)
                        last.then_inc(tg_projected, 1)
                        return tg_copied, i

                    def transpose_u():
                        pe.wait_ge(*extra_free)
                        pe.wait_ge(u_ready, i)
                        transpose_tiles(extra_ps, u).then_inc(u_transposed, 1)
                        return ut_ready, i

                    def project_z():
                        pe.wait_ge(*extra_free)
                        for j in range(NT):
                            nc.tensor.matmul(tile(extra_ps, j), tile(x1t, j), ffn[:, F_W:F_W + D],
                                             start=True, stop=False)
                            last = nc.tensor.matmul(tile(extra_ps, j), tile(ut, j), ffn[:, F_V:F_V + D],
                                                    start=False, stop=True)
                        last.then_inc(z_projected, 1)
                        return z_copied, i + 1

                    if p == PAIRS - 1 and mode == FIRST:
                        pe.wait_ge(w_lo_ready["o"], 1)
                        pe.wait_ge(ffn_scaled, 1)

                    if p == 0 and has_scores(mode):
                        extra_free = extra_v(0)
                    if p == 6 and has_next(mode):
                        extra_free = transpose_xn()
                    if has_scores(mode):
                        scores()
                    if p == 2 and has_previous(mode):
                        extra_free = output_projection(range(2, 4))
                    if p == 3 and has_previous(mode):
                        extra_free = output_projection(range(6, 8))
                    if p == 5 and has_scores(mode):
                        extra_free = extra_v(2)
                    if has_next_qk(p, mode):
                        next_qk()
                    if p == 2 and has_previous(mode):
                        extra_free = output_projection(range(4, 6))
                    if p == 3 and has_previous(mode):
                        extra_free = transpose_y()
                    if p == 6 and has_previous(mode):
                        extra_free = project_tg()
                    if p == 7 and has_previous(mode):
                        extra_free = transpose_u()
                    if has_trailing(p, mode, 1):
                        transpose_probs(0)
                    if p == 0 and has_scores(mode):
                        extra_free = extra_v(1)
                    if p == 1 and has_previous(mode):
                        extra_free = output_projection(range(0, 2))
                    if has_trailing(p, mode, 1):
                        transpose_probs(1)
                    if p == 3 and has_scores(mode):
                        extra_free = extra_v(3)
                    if p == 5 and has_previous(mode):
                        extra_free = transpose_x1n()
                    if p == 7 and has_previous(mode):
                        extra_free = project_z()
                    if has_trailing(p, mode, 2):
                        probs_v()

            run(pe, body)

        @block.scalar
        def _(act):
            def qk_hi(pair, par, g):
                act.wait_ge(qk_projected, g + 1)
                nc.scalar.activation(q_hi[par][:, :], qk_ps[:, 0:T], ACT.Identity,
                                     bias=bias[:, B_Q + pair:B_Q + pair + 1])
                nc.scalar.activation(k_hi[par][:, :], qk_ps[:, T:2 * T], ACT.Identity,
                                     bias=bias[:, B_K + pair:B_K + pair + 1]).then_inc(qk_hi_ready, 1)

            act.wait_ge(bias_loaded, 16)
            nc.scalar.mul(bias[:, B_Q:B_Q + PAIRS], bias[:, B_Q:B_Q + PAIRS],
                          SCORE_SCALE).then_inc(bias_scaled, 1)

            def weight_hi(n, cols, loaded, ready):
                act.wait_ge(loaded[n], 16)
                nc.scalar.mul(w_hi[n][:, cols], stage[n][:, cols],
                              SCORE_SCALE if n == "q" else 1.0).then_inc(ready[n], 1)

            for n in "qk":
                weight_hi(n, early, early_loaded, early_hi_ready)
            act.wait_ge(x_transposed, 1)
            nc.scalar.copy(xt_hi[:, :], extra_ps[:, 0:T]).then_inc(xt_hi_ready, 1)
            weight_hi("v", every, w_loaded, w_hi_ready)
            act.wait_ge(bias_scaled, 1)
            qk_hi(0, 0, 0)
            weight_hi("q", late, w_loaded, w_hi_ready)
            qk_hi(1, 1, 1)
            weight_hi("k", late, w_loaded, w_hi_ready)

            def body(i, mode):
                for p in range(PAIRS):
                    g = PAIRS * i + p
                    par = p % 2

                    def exponentials(h):
                        act.wait_ge(max_ready[h], g + 1)
                        after(act, probs_transposed[h], g - 1)
                        for j in range(NT):
                            last = nc.scalar.activation(
                                probs[par][h][:, j, :], scores_ps[h][par][:, j * T:(j + 1) * T],
                                ACT.Exp, bias=neg_max[par][h][:, j:j + 1],
                                accum_out=row_sum[par][h][:, j:j + 1])
                        last.then_inc(exp_ready[h], 1)

                    def copy_probs_t(lag):
                        act.wait_ge(probs_transposed[0], g - lag + 1)
                        after(act, o_projected, g - lag - 1)
                        nc.scalar.copy(probs_t[(p - lag) % 2][0][:, :, :].rearrange("p s q -> p (s q)"),
                                       probs_t_ps[0][:, :]).then_inc(probs_t_copied[0], 1)

                    def attention_hi(lag):
                        pair = (p - lag) % PAIRS
                        act.wait_ge(o_projected, g - lag + 1)
                        nc.scalar.activation(o_hi[:, pair, :], o_ps[:, 0:T], ACT.Identity,
                                             bias=bias[:, B_V + pair:B_V + pair + 1]
                                             ).then_inc(o_hi_ready, 1)

                    def copy_v(quarter):
                        act.wait_ge(v_projected[quarter], i + 1)
                        half = quarter // 2
                        nc.scalar.copy(v_sb[:, quarter % 2, half * HALF:(half + 1) * HALF],
                                       extra_ps[:, :]).then_inc(v_copied[quarter], 1)

                    def copy_yt():
                        act.wait_ge(yt_projected, i)
                        nc.scalar.activation(yt[:, :], extra_ps[:, 0:T], ACT.Identity,
                                             bias=bias[:, B_O:B_O + 1]).then_inc(yt_ready, 1)

                    def copy_ut():
                        act.wait_ge(u_transposed, i)
                        nc.scalar.copy(ut[:, :], extra_ps[:, 0:T]).then_inc(ut_ready, 1)

                    def xt_high():
                        act.wait_ge(x_transposed, i + 2)
                        nc.scalar.copy(xt_hi[:, :], extra_ps[:, 0:T]).then_inc(xt_hi_ready, 1)

                    def gate_exponentials():
                        act.wait_ge(gate_max_ready, i)
                        for j in range(NT):
                            last = nc.scalar.activation(gate_exp[:, j, :], tg[:, j, E * R:TG], ACT.Exp,
                                                        bias=gate_neg_max[:, j:j + 1],
                                                        accum_out=gate_sum[:, j:j + 1])
                        last.then_inc(gate_exp_ready, 1)

                    def copy_z():
                        act.wait_ge(z_projected, i)
                        nc.scalar.copy(z[:, :], extra_ps[:, 0:T]).then_inc(z_copied, 1)

                    if mode == FIRST and p == 1:
                        weight_hi("o", every, w_loaded, w_hi_ready)
                        act.wait_ge(ffn_loaded, 16)
                        nc.scalar.mul(ffn[:, F_V:F_V + D], ffn[:, F_V:F_V + D],
                                      LORA_SCALE).then_inc(ffn_scaled, 1)

                    if p == 7 and has_previous(mode):
                        gate_exponentials()
                    if has_trailing(p, mode, 3):
                        attention_hi(3)
                    if has_trailing(p, mode, 2):
                        copy_probs_t(2)
                    if p == 0 and has_scores(mode):
                        copy_v(0)
                    if p == 1 and has_scores(mode):
                        copy_v(1)
                    if p == 3 and has_previous(mode):
                        copy_yt()
                    if p == 5 and has_scores(mode):
                        copy_v(2)
                    if p == 7 and has_previous(mode):
                        copy_ut()
                    if has_scores(mode):
                        exponentials(0)
                    if has_next_qk(p, mode):
                        qk_hi((p + 2) % PAIRS, par, g + 2)
                    if p == 7 and has_previous(mode):
                        copy_z()
                    if has_scores(mode):
                        exponentials(1)
                    if p == 3 and has_scores(mode):
                        copy_v(3)
                    if p == 5 and has_next(mode):
                        xt_high()

            run(act, body)

        @block.vector
        def _(dve):
            def f32(ap):
                return ap.bitcast(F32)

            def qk_lo(pair, par, g):
                dve.wait_ge(qk_hi_ready, g + 1)
                nc.vector.scalar_tensor_tensor(q_lo[par][:, :], qk_ps[:, 0:T],
                                               bias[:, B_Q + pair:B_Q + pair + 1],
                                               f32(q_hi[par][:, :]), ALU.add, ALU.subtract)
                nc.vector.scalar_tensor_tensor(k_lo[par][:, :], qk_ps[:, T:2 * T],
                                               bias[:, B_K + pair:B_K + pair + 1],
                                               f32(k_hi[par][:, :]), ALU.add, ALU.subtract
                                               ).then_inc(qk_lo_ready, 1)

            def ln_stats(ln, src, count):
                for j in range(NT):
                    last = nc.vector.bn_stats(stats[ln][:, j, :], tile(src, j))
                last.then_inc(stats_ready[ln], 1)
                dve.wait_ge(stats_ready[ln], count)
                nc.vector.tensor_copy(stats_seen[:, :], stats[ln][:, NT - 1, 0:1])
                for j in range(NT):
                    last = nc.vector.bn_aggr(mean_var[ln][:, j, :], stats[ln][:, j, :])
                last.then_inc(mean_var_ready[ln], 1)
                dve.wait_ge(mean_var_ready[ln], count)
                nc.vector.tensor_scalar(var_eps[ln][:, :], mean_var[ln][:, :, 1], EPS, None,
                                        ALU.add).then_inc(var_eps_ready[ln], 1)

            def ln_apply(ln, dst, src):
                for j in range(NT):
                    last = nc.vector.tensor_scalar(tile(dst, j), tile(src, j), mean_var[ln][:, j, 0:1],
                                                   rstd[ln][:, j:j + 1], ALU.subtract, ALU.mult)
                return last

            nc.vector.memset(stats_seen[:, :], 0.0).then_inc(z_copied, 1)
            dve.wait_ge(x_loaded[0], 16)
            ln_stats(LN_X, x_all[:, 0:NT * D], 1)
            dve.wait_ge(rstd_ready[LN_X], 1)
            ln_apply(LN_X, xn, x_all).then_inc(xn_ready, 1)

            def weight_lo(n, cols, hi_ready, ready):
                dve.wait_ge(hi_ready[n], 1)
                nc.vector.scalar_tensor_tensor(w_lo[n][:, cols], stage[n][:, cols],
                                               SCORE_SCALE if n == "q" else 1.0,
                                               f32(w_hi[n][:, cols]), ALU.mult, ALU.subtract
                                               ).then_inc(ready[n], 1)

            for n in "qk":
                weight_lo(n, early, early_hi_ready, early_lo_ready)
            dve.wait_ge(xt_hi_ready, 1)
            nc.vector.tensor_tensor(xt_lo[:, :], extra_ps[:, 0:T], f32(xt_hi[:, :]),
                                    ALU.subtract).then_inc(xt_lo_ready, 1)

            weight_lo("v", every, w_hi_ready, w_lo_ready)
            qk_lo(0, 0, 0)
            weight_lo("q", late, w_hi_ready, w_lo_ready)
            qk_lo(1, 1, 1)
            weight_lo("k", late, w_hi_ready, w_lo_ready)

            def body(i, mode):
                for p in range(PAIRS):
                    g = PAIRS * i + p
                    par = p % 2

                    def row_max(h):
                        dve.wait_ge(scores_ready[h], g + 1)
                        nc.vector.tensor_reduce(
                            neg_max[par][h][:, :],
                            scores_ps[h][par][:, :].rearrange("p (j s) -> p j s", j=NT),
                            AX.X, ALU.max, negate=True).then_inc(max_ready[h], 1)

                    def invert_sum(h, g, par):
                        dve.wait_ge(exp_ready[h], g + 1)
                        nc.vector.reciprocal(inv_sum[par][h][:, :],
                                             row_sum[par][h][:, :]).then_inc(inv_ready[h], 1)

                    def attention_lo(lag):
                        pair = (p - lag) % PAIRS
                        dve.wait_ge(o_hi_ready, g - lag + 1)
                        nc.vector.scalar_tensor_tensor(o_lo[:, pair, :], o_ps[:, 0:T],
                                                       bias[:, B_V + pair:B_V + pair + 1],
                                                       f32(o_hi[:, pair, :]), ALU.add, ALU.subtract
                                                       ).then_inc(o_lo_ready, 1)

                    def copy_probs_t(lag):
                        dve.wait_ge(probs_transposed[1], g - lag + 1)
                        after(dve, o_projected, g - lag - 1)
                        nc.vector.tensor_copy(probs_t[(p - lag) % 2][1][:, :, :].rearrange("p s q -> p (s q)"),
                                              probs_t_ps[1][:, :]).then_inc(probs_t_copied[1], 1)

                    def norm_y():
                        dve.wait_ge(rstd_ready[LN_Y], i)
                        ln_apply(LN_Y, y, y).then_inc(y_normed, 1)
                        dve.wait_ge(y_normed, i)
                        nc.vector.tensor_tensor(x1[:, :], y[:, :], x_tiles(i - 1),
                                                ALU.add).then_inc(x1_ready, 1)

                    def norm_x1():
                        dve.wait_ge(rstd_ready[LN_X1], i)
                        ln_apply(LN_X1, x1n, x1).then_inc(x1n_ready, 1)

                    def xt_low():
                        dve.wait_ge(xt_hi_ready, i + 2)
                        nc.vector.tensor_tensor(xt_lo[:, :], extra_ps[:, 0:T], f32(xt_hi[:, :]),
                                                ALU.subtract).then_inc(xt_lo_ready, 1)

                    def copy_y():
                        dve.wait_ge(y_transposed, i)
                        nc.vector.tensor_copy(y[:, :], extra_ps[:, 0:T]).then_inc(y_copied, 1)

                    def copy_tg():
                        dve.wait_ge(tg_projected, i)
                        nc.vector.tensor_copy(tg[:, :, :].rearrange("p j n -> p (j n)"),
                                              extra_ps[:, 0:NT * TG]).then_inc(tg_copied, 1)

                    def gate_max():
                        dve.wait_ge(tg_copied, i)
                        nc.vector.tensor_reduce(gate_neg_max[:, :], tg[:, :, E * R:TG], AX.X, ALU.max,
                                                negate=True).then_inc(gate_max_ready, 1)

                    def apply_gate():
                        dve.wait_ge(gate_exp_ready, i)
                        nc.vector.reciprocal(gate_inv[:, :], gate_sum[:, :]).then_inc(gate_inv_ready, 1)
                        dve.wait_ge(gate_inv_ready, i)
                        for j in range(NT):
                            last = nc.vector.tensor_scalar(gate[:, j, :], gate_exp[:, j, :],
                                                           gate_inv[:, j:j + 1], None, ALU.mult)
                        last.then_inc(gate_ready, 1)
                        dve.wait_ge(gate_ready, i)
                        for j in range(NT):
                            last = nc.vector.tensor_tensor(
                                tile(u, j).rearrange("p (e r) -> p e r", e=E),
                                tg[:, j, 0:E * R].rearrange("p (e r) -> p e r", e=E),
                                gate[:, j, :].unsqueeze(2).to_broadcast([P, E, R]), ALU.mult)
                        last.then_inc(u_ready, 1)

                    def stats_x():
                        dve.wait_ge(x_loaded[1 if mode == FIRST else 2], 16)
                        ln_stats(LN_X, x_tiles(i + 1), i + 2)

                    def stats_y():
                        dve.wait_ge(y_copied, i)
                        ln_stats(LN_Y, y, i)

                    def stats_x1():
                        dve.wait_ge(x1_ready, i)
                        ln_stats(LN_X1, x1, i)

                    def stats_z():
                        dve.wait_ge(z_copied, i + 1)
                        ln_stats(LN_Z, z, i)

                    def copy_x1t():
                        dve.wait_ge(x1_transposed, i)
                        nc.vector.tensor_copy(x1t[:, :], extra_ps[:, 0:T]).then_inc(x1t_ready, 1)

                    if mode == FIRST and p == 2:
                        weight_lo("o", every, w_hi_ready, w_lo_ready)

                    if has_trailing(p, mode, 1):
                        invert_sum(1, g - 1, 1 - par)
                    if p == 1 and has_next(mode):
                        stats_x()
                    if p == 4 and has_previous(mode):
                        norm_y()
                    if p == 6 and has_next(mode):
                        xt_low()
                    if p == 7 and has_previous(mode):
                        apply_gate()
                    if has_scores(mode):
                        row_max(0)
                    if p == 5 and has_previous(mode):
                        norm_x1()
                    if has_trailing(p, mode, 3):
                        attention_lo(3)
                    if p == 4 and has_previous(mode):
                        stats_x1()
                    if has_scores(mode):
                        row_max(1)
                    if p == 3 and has_previous(mode):
                        copy_y()
                    if p == 5 and has_previous(mode):
                        copy_x1t()
                    if p == 6 and has_previous(mode):
                        copy_tg()
                    if p == 6 and has_previous(mode):
                        gate_max()
                    if has_scores(mode):
                        invert_sum(0, g, par)
                    if p == 3 and has_previous(mode):
                        stats_y()
                    if has_trailing(p, mode, 1):
                        copy_probs_t(1)
                    if has_next_qk(p, mode):
                        qk_lo((p + 2) % PAIRS, par, g + 2)
                    if p == 7 and has_previous(mode):
                        stats_z()

            run(dve, body)

        @block.gpsimd
        def _(pool):
            def per_tile(column):
                return column.unsqueeze(2).to_broadcast([P, NT, D])

            def tiles(ap):
                return ap.rearrange("p (j d) -> p j d", j=NT)

            def ln_rstd(ln, count):
                pool.wait_ge(var_eps_ready[ln], count)
                nc.gpsimd.tensor_tensor(rstd[ln][:, :], var_eps[ln][:, :], neg_half[:, :],
                                        ALU.pow).then_inc(rstd_ready[ln], 1)

            def norm_x(b):
                ln_rstd(LN_X, b + 1)
                nc.gpsimd.tensor_tensor(tiles(xn[:, :]), tiles(x_tiles(b)),
                                        per_tile(mean_var[LN_X][:, :, 0]),
                                        ALU.subtract).then_inc(xn_centred, 1)
                pool.wait_ge(rstd_ready[LN_X], b + 1)
                pool.wait_ge(xn_centred, b)
                nc.gpsimd.tensor_tensor(tiles(xn[:, :]), tiles(xn[:, :]), per_tile(rstd[LN_X][:, :]),
                                        ALU.mult).then_inc(xn_ready, 1)

            nc.gpsimd.memset(neg_half[:, :], -0.5)
            nc.gpsimd.memset(ident[:, :], 0.0).then_inc(zeroed, 1)
            pool.wait_ge(zeroed, 1)
            nc.gpsimd.affine_select(out=ident[:, :], in_=ident[:, :], compare_op=ALU.not_equal, fill=1.0,
                                    base=0, pattern=[[-1, P]], channel_multiplier=1
                                    ).then_inc(constants_ready, 1)
            ln_rstd(LN_X, 1)

            def body(i, mode):
                for p in range(PAIRS):
                    g = PAIRS * i + p
                    par = p % 2

                    def scale_probs(h):
                        pool.wait_ge(inv_ready[h], g + 1)
                        nc.gpsimd.tensor_tensor(
                            probs[par][h][:, :, :], probs[par][h][:, :, :],
                            inv_sum[par][h][:, :].unsqueeze(2).to_broadcast([P, NT, T]),
                            ALU.mult).then_inc(probs_ready[h], 1)

                    def norm_z():
                        ln_rstd(LN_Z, i)
                        nc.gpsimd.tensor_tensor(tiles(z[:, :]), tiles(z[:, :]),
                                                per_tile(mean_var[LN_Z][:, :, 0]),
                                                ALU.subtract).then_inc(z_centred, 1)
                        pool.wait_ge(rstd_ready[LN_Z], i)
                        pool.wait_ge(z_centred, i)
                        nc.gpsimd.tensor_tensor(tiles(z[:, :]), tiles(z[:, :]), per_tile(rstd[LN_Z][:, :]),
                                                ALU.mult).then_inc(z_normed, 1)
                        pool.wait_ge(z_normed, i)
                        nc.gpsimd.tensor_tensor(x_tiles(i - 1), z[:, :], x1[:, :],
                                                ALU.add).then_inc(out_ready, 1)

                    if p == 4 and has_previous(mode):
                        ln_rstd(LN_X1, i)
                    if has_scores(mode):
                        scale_probs(0)
                    if has_scores(mode):
                        scale_probs(1)
                    if p == 1 and has_next(mode):
                        norm_x(i + 1)
                    if p == 2 and has_previous(mode):
                        ln_rstd(LN_Y, i)
                    if p == 7 and has_previous(mode):
                        norm_z()

            run(pool, body)


def kernel(L0_attn_x, L0_attn_W_Q, L0_attn_b_Q, L0_attn_W_K, L0_attn_b_K, L0_attn_W_V, L0_attn_b_V,
           L0_attn_W_O, L0_attn_b_O, L0_ffn_weight, L0_ffn_gate_w, L0_ffn_lora_U, L0_ffn_lora_V):
    import numpy as np
    import concourse.bacc as bacc
    from concourse import mybir as mb
    from concourse.bass_utils import run_bass_kernel_spmd

    def head_weight(w):
        return np.asarray(w).reshape(H * DH, D).T

    def head_bias(b):
        return np.asarray(b).reshape(PAIRS, P).T

    laid_out = {
        "x": np.asarray(L0_attn_x),
        "w_q": head_weight(L0_attn_W_Q),
        "w_k": head_weight(L0_attn_W_K),
        "w_v": head_weight(L0_attn_W_V),
        "w_o": np.asarray(L0_attn_W_O).transpose(0, 2, 1).reshape(PAIRS, P, D).transpose(1, 0, 2)
                 .reshape(P, PAIRS * D),
        "biases": np.concatenate([head_bias(L0_attn_b_Q), head_bias(L0_attn_b_K),
                                  head_bias(L0_attn_b_V), np.asarray(L0_attn_b_O).reshape(D, 1)], axis=1),
        "ffn_w": np.concatenate([np.asarray(L0_ffn_weight).T,
                                 np.asarray(L0_ffn_lora_U).reshape(E * R, D).T,
                                 np.asarray(L0_ffn_gate_w).T,
                                 np.asarray(L0_ffn_lora_V).transpose(0, 2, 1).reshape(E * R, D)], axis=1),
    }
    nc = bacc.Bacc("TRN2", target_bir_lowering=False, num_devices=1)
    arrays, args = {}, []
    for name, a in laid_out.items():
        a = np.ascontiguousarray(a)
        arrays[f"in_{name}"] = a
        args.append(nc.dram_tensor(f"in_{name}", a.shape, mb.dt.from_np(a.dtype), kind="ExternalInput").ap())
    out = nc.dram_tensor("out", (B, T, D), mb.dt.float32, kind="ExternalOutput").ap()
    transformer_layer(nc, *args, out)
    return run_bass_kernel_spmd(nc, [arrays], core_ids=[0]).results[0]["out"]
```
